# Optimizing a Trainium2 kernel written in Bass

```python
import numpy as np
import jax
import jax.numpy as jnp

def _softmax(x, axis=-1):
    return jax.nn.softmax(x, axis=axis)
def _gelu(x):
    return jax.nn.gelu(x, approximate=True)
def _silu(x):
    return jax.nn.silu(x)
def _sigmoid(x):
    return jax.nn.sigmoid(x)
def _layernorm(x, axis=-1, eps=1e-5):
    m = jnp.mean(x, axis=axis, keepdims=True)
    v = jnp.var(x, axis=axis, keepdims=True)
    return (x - m) / jnp.sqrt(v + eps)
def _scatter_add(tgt, idx, src, axis=0):
    return tgt.at[idx].add(src)
def _segment_sum(src, seg, n):
    return jax.ops.segment_sum(src, seg, n)

kernel_name = 'mk_rec_standalone_d1_rec_27464e'

def setup_inputs(seed: int = 0):
    np.random.seed(seed)
    _w = jnp.asarray
    def _rec_inputs():
        import jax
        import jax.numpy as jnp
        _rk = jax.random.key(seed)
        r_initial = -0.000125008 + 0.999885 * jax.random.normal(jax.random.fold_in(_rk, 1), (16384, 2048), jnp.float32)
        r_X = -1.52775e-05 + 0.999936 * jax.random.normal(jax.random.fold_in(_rk, 2), (16384, 2048), jnp.float32)
        return r_initial, r_X
    r_initial, r_X = _rec_inputs()
    def _L0_rec_setup():
        import jax, jax.numpy as jnp
        import numpy as np
        B, D = (16384, 2048)
        key = jax.random.key(seed)
        k1, k2, k3 = jax.random.split(key, 3)
        stdv = 1.0 / np.sqrt(D)
        initial = jax.random.normal(k1, (B, D), dtype=jnp.float32)
        X = jax.random.normal(k2, (B, D), dtype=jnp.float32)
        alphas = jax.random.uniform(k3, (D, 1), dtype=jnp.float32, minval=-stdv, maxval=stdv)
        bias = jnp.zeros((D,), dtype=jnp.float32)
        return {'initial': initial, 'X': X, 'alphas': alphas, 'bias': bias}
    _L0_rec_all = _L0_rec_setup()
    _L0_rec_in = {k: v for k, v in _L0_rec_all.items() if k in ('alphas', 'bias', )}
    del _L0_rec_all

    return {
        "r_initial": r_initial,
        "r_X": r_X,
        "L0_rec_alphas": _L0_rec_in["alphas"],
        "L0_rec_bias": _L0_rec_in["bias"],
    }

def reference(r_initial, r_X, L0_rec_alphas, L0_rec_bias):
    import jax
    import jax.numpy as jnp
    def _L0_rec_ref(initial, X, alphas, bias):
        import jax, jax.numpy as jnp
        import numpy as np
        B, D = (16384, 2048)
        scale = X @ alphas
        return initial * scale + X + bias

    y = _L0_rec_ref(r_initial, r_X, L0_rec_alphas, L0_rec_bias)
    return y


_drawn_inputs = setup_inputs


def setup_inputs(seed=0):
    import zlib

    import numpy as np

    out = dict(_drawn_inputs(seed))
    spreads = {'L0_rec_bias': (0.0, 0.1)}
    factors = {}
    for name, (base, spread) in spreads.items():
        noise = np.random.default_rng([zlib.crc32(name.encode()), seed]).standard_normal(out[name].shape)
        drawn = base * np.exp(spread * noise) if base else spread * noise
        out[name] = jnp.asarray(drawn.astype(out[name].dtype))
    for name, factor in factors.items():
        out[name] = (out[name] * factor).astype(out[name].dtype)
    return out
```

```python
from contextlib import ExitStack

import concourse.bass as bass
from concourse import mybir
from concourse.alu_op_type import AluOpType as ALU

F32 = mybir.dt.float32
PARTITIONS = 128
ROWS = 2
SLOTS = 4
BANK = 512
DMA_DONE = 16


def rec_scale_program(nc, initial, X, alphas, bias, out):
    B, D = X.shape
    TILE_ROWS = PARTITIONS * ROWS
    TILES = B // TILE_ROWS
    BANKS = D // BANK
    assert B % TILE_ROWS == 0 and D % BANK == 0 and TILES % SLOTS == 0 and 2 * BANKS <= 8
    PASSES = TILES // SLOTS

    with ExitStack() as ctx:
        def sbuf(name, shape):
            return ctx.enter_context(nc.sbuf_tensor(name, shape, F32))

        def sem(name):
            return ctx.enter_context(nc.semaphore(name))

        x_tiles = sbuf("x_tiles", [PARTITIONS, SLOTS, ROWS, D])
        init_tiles = sbuf("init_tiles", [PARTITIONS, SLOTS, ROWS, D])
        products = sbuf("products", [PARTITIONS, D])
        scales = sbuf("scales", [PARTITIONS, SLOTS, ROWS])
        ones = sbuf("ones", [1, PARTITIONS])
        alphas_row = sbuf("alphas_row", [1, D])
        bias_row = sbuf("bias_row", [1, D])
        alphas_all = ctx.enter_context(nc.psum_tensor("alphas_all", [PARTITIONS, D], F32))
        bias_all = ctx.enter_context(nc.psum_tensor("bias_all", [PARTITIONS, D], F32))

        alphas_loaded, bias_loaded = sem("alphas_loaded"), sem("bias_loaded")
        ones_ready = sem("ones_ready")
        alphas_spread, bias_spread = sem("alphas_spread"), sem("bias_spread")
        x_loaded = [sem(f"x_loaded{s}") for s in range(SLOTS)]
        init_loaded = [sem(f"init_loaded{s}") for s in range(SLOTS)]
        stored = [sem(f"stored{s}") for s in range(SLOTS)]
        dots_done = sem("dots_done")
        shifts_done = sem("shifts_done")
        mixes_done = sem("mixes_done")

        def x_dram(row0):
            return X[bass.ds(row0, TILE_ROWS), :].rearrange("(p r) d -> p r d", p=PARTITIONS)

        def init_dram(row0):
            return initial[bass.ds(row0, TILE_ROWS), :].rearrange("(p r) d -> p r d", p=PARTITIONS)

        def out_dram(row0):
            return out[bass.ds(row0, TILE_ROWS), :].rearrange("(p r) d -> p r d", p=PARTITIONS)

        block = ctx.enter_context(nc.Block())

        @block.sync
        def _(sp):
            sp.dma_start(alphas_row[:], alphas.rearrange("d a -> a d")).then_inc(alphas_loaded, DMA_DONE)
            sp.dma_start(bias_row[:], bias.rearrange("(a d) -> a d", a=1)).then_inc(bias_loaded, DMA_DONE)
            for s in range(SLOTS):
                sp.dma_start(x_tiles[:, s], x_dram(s * TILE_ROWS)).then_inc(x_loaded[s], DMA_DONE)
                sp.dma_start(init_tiles[:, s], init_dram(s * TILE_ROWS)).then_inc(init_loaded[s], DMA_DONE)
            with sp.Fori(1, PASSES) as n:
                for s in range(SLOTS):
                    row0 = n * (SLOTS * TILE_ROWS) + s * TILE_ROWS
                    sp.wait_ge(mixes_done, n * (SLOTS * ROWS) + (s + 1 - SLOTS) * ROWS)
                    sp.dma_start(x_tiles[:, s], x_dram(row0)).then_inc(x_loaded[s], DMA_DONE)
                    sp.wait_ge(stored[s], n * DMA_DONE)
                    sp.dma_start(init_tiles[:, s], init_dram(row0)).then_inc(init_loaded[s], DMA_DONE)

        @block.tensor
        def _(pe):
            pe.wait_ge(ones_ready, 1)
            pe.wait_ge(alphas_loaded, DMA_DONE)
            for b in range(BANKS):
                cols = slice(b * BANK, (b + 1) * BANK)
                nc.tensor.matmul(alphas_all[:, cols], ones[:], alphas_row[:, cols],
                                 start=True, stop=True).then_inc(alphas_spread, 1)
            pe.wait_ge(bias_loaded, DMA_DONE)
            for b in range(BANKS):
                cols = slice(b * BANK, (b + 1) * BANK)
                nc.tensor.matmul(bias_all[:, cols], ones[:], bias_row[:, cols],
                                 start=True, stop=True).then_inc(bias_spread, 1)

        @block.vector
        def _(dve):
            nc.vector.memset(ones[:], 1.0).then_inc(ones_ready, 1)
            dve.wait_ge(alphas_spread, BANKS)
            dve.wait_ge(bias_spread, BANKS)
            with dve.Fori(0, PASSES) as n:
                for s in range(SLOTS):
                    dve.wait_ge(x_loaded[s], n * DMA_DONE + DMA_DONE)
                    for r in range(ROWS):
                        done = n * (SLOTS * ROWS) + (s * ROWS + r)
                        nc.vector.tensor_tensor_reduce(
                            out=products[:], in0=x_tiles[:, s, r], in1=alphas_all[:], scale=1.0,
                            scalar=0.0, op0=ALU.mult, op1=ALU.add,
                            accum_out=scales[:, s, r:r + 1]).then_inc(dots_done, 1)
                        nc.vector.tensor_tensor(x_tiles[:, s, r], x_tiles[:, s, r], bias_all[:],
                                                ALU.add).then_inc(shifts_done, 1)
                        if r == 0:
                            dve.wait_ge(init_loaded[s], n * DMA_DONE + DMA_DONE)
                        dve.wait_ge(dots_done, done + 1)
                        dve.wait_ge(shifts_done, done + 1)
                        nc.vector.scalar_tensor_tensor(
                            out=init_tiles[:, s, r], in0=init_tiles[:, s, r],
                            scalar=scales[:, s, r:r + 1], in1=x_tiles[:, s, r],
                            op0=ALU.mult, op1=ALU.add).then_inc(mixes_done, 1)

        @block.scalar
        def _(act):
            with act.Fori(0, PASSES) as n:
                for s in range(SLOTS):
                    act.wait_ge(mixes_done, n * (SLOTS * ROWS) + (s + 1) * ROWS)
                    act.dma_start(out_dram(n * (SLOTS * TILE_ROWS) + s * TILE_ROWS),
                                  init_tiles[:, s]).then_inc(stored[s], DMA_DONE)
            for s in range(SLOTS):
                act.wait_ge(stored[s], PASSES * DMA_DONE)


_INS = ['r_initial', 'r_X', 'L0_rec_alphas', 'L0_rec_bias']
_OUTS = [((16384, 2048), 'float32')]


def kernel(**inputs):
    import numpy as _np
    import concourse.bacc as _bacc
    from concourse import mybir as _mybir
    from concourse.bass_utils import run_bass_kernel_spmd as _run

    nc = _bacc.Bacc("TRN2", target_bir_lowering=False, num_devices=1)
    arrays, args = {}, []
    for name in _INS:
        a = _np.ascontiguousarray(inputs[name])
        arrays[f"in_{name}_dram"] = a
        args.append(nc.dram_tensor(f"in_{name}_dram", a.shape, _mybir.dt.from_np(a.dtype), kind="ExternalInput").ap())
    for i, (shape, dtype) in enumerate(_OUTS):
        dt = _mybir.dt.from_np(_np.dtype(dtype))
        args.append(nc.dram_tensor(f"out_{i}_dram", shape, dt, kind="ExternalOutput").ap())
    rec_scale_program(nc, *args)
    r = _run(nc, [arrays], core_ids=[0])
    got = tuple(r.results[0][f"out_{i}_dram"] for i in range(len(_OUTS)))
    return got[0]
```

```python
from contextlib import ExitStack

import concourse.bass as bass
from concourse import mybir
from concourse.alu_op_type import AluOpType as ALU

F32 = mybir.dt.float32
PARTITIONS = 128
ROWS = 2
SLOTS = 4
BANK = 512
PIECES = 2
DMA_DONE = 16


def rec_scale_program(nc, initial, X, alphas, bias, out):
    B, D = X.shape
    TILE_ROWS = PARTITIONS * ROWS
    TILES = B // TILE_ROWS
    BANKS = D // BANK
    assert B % TILE_ROWS == 0 and D % BANK == 0 and D % PIECES == 0 and TILES % SLOTS == 0
    assert 2 * BANKS <= 8
    PASSES = TILES // SLOTS

    with ExitStack() as ctx:
        def sbuf(name, shape):
            return ctx.enter_context(nc.sbuf_tensor(name, shape, F32))

        def sem(name):
            return ctx.enter_context(nc.semaphore(name))

        x_tiles = sbuf("x_tiles", [PARTITIONS, SLOTS, ROWS, D])
        init_tiles = sbuf("init_tiles", [PARTITIONS, SLOTS, ROWS, D])
        products = sbuf("products", [PARTITIONS, ROWS, D])
        scales = sbuf("scales", [PARTITIONS, SLOTS, ROWS])
        ones = sbuf("ones", [1, PARTITIONS])
        alphas_row = sbuf("alphas_row", [1, D])
        bias_row = sbuf("bias_row", [1, D])
        alphas_all = ctx.enter_context(nc.psum_tensor("alphas_all", [PARTITIONS, D], F32))
        bias_all = ctx.enter_context(nc.psum_tensor("bias_all", [PARTITIONS, D], F32))

        alphas_loaded, bias_loaded = sem("alphas_loaded"), sem("bias_loaded")
        ones_ready = sem("ones_ready")
        alphas_spread, bias_spread = sem("alphas_spread"), sem("bias_spread")
        x_loaded = [sem(f"x_loaded{s}") for s in range(SLOTS)]
        init_loaded = [sem(f"init_loaded{s}") for s in range(SLOTS)]
        last_init_loaded = [sem(f"last_init_loaded{i}") for i in range(ROWS * PIECES)]
        last_stored = sem("last_stored")
        last_mixes_done = sem("last_mixes_done")
        stored = [sem(f"stored{s}") for s in range(SLOTS)]
        dots_done = sem("dots_done")
        shifts_done = sem("shifts_done")
        mixes_done = sem("mixes_done")

        def tile_of(dram, row0):
            return dram[bass.ds(row0, TILE_ROWS), :].rearrange("(p r) d -> p r d", p=PARTITIONS)

        LAST = SLOTS - 1
        LAST_ROW0 = (TILES - 1) * TILE_ROWS
        PIECE = D // PIECES

        def piece(c):
            return slice(c * PIECE, (c + 1) * PIECE)

        block = ctx.enter_context(nc.Block())

        @block.sync
        def _(sp):
            def load_again(n, s):
                row0 = n * (SLOTS * TILE_ROWS) + s * TILE_ROWS
                sp.wait_ge(mixes_done, n * (SLOTS * ROWS) + (s + 1 - SLOTS) * ROWS)
                sp.dma_start(x_tiles[:, s], tile_of(X, row0)).then_inc(x_loaded[s], DMA_DONE)
                sp.wait_ge(stored[s], n * DMA_DONE)
                sp.dma_start(init_tiles[:, s], tile_of(initial, row0)).then_inc(init_loaded[s], DMA_DONE)

            for s in range(SLOTS):
                sp.dma_start(x_tiles[:, s], tile_of(X, s * TILE_ROWS)).then_inc(x_loaded[s], DMA_DONE)
                sp.dma_start(init_tiles[:, s], tile_of(initial, s * TILE_ROWS)).then_inc(init_loaded[s], DMA_DONE)
            with sp.Fori(1, PASSES - 1) as n:
                for s in range(SLOTS):
                    load_again(n, s)
            for s in range(SLOTS - 1):
                load_again(PASSES - 1, s)
            sp.wait_ge(mixes_done, (TILES - SLOTS) * ROWS)
            sp.dma_start(x_tiles[:, LAST], tile_of(X, LAST_ROW0)).then_inc(x_loaded[LAST], DMA_DONE)
            sp.wait_ge(stored[LAST], (PASSES - 1) * DMA_DONE)
            for r in range(ROWS):
                for c in range(PIECES):
                    sp.dma_start(init_tiles[:, LAST, r, piece(c)],
                                 tile_of(initial, LAST_ROW0)[:, r, piece(c)]).then_inc(
                                     last_init_loaded[r * PIECES + c], DMA_DONE)

        @block.tensor
        def _(pe):
            pe.wait_ge(ones_ready, 1)
            pe.wait_ge(alphas_loaded, DMA_DONE)
            for b in range(BANKS):
                cols = slice(b * BANK, (b + 1) * BANK)
                nc.tensor.matmul(alphas_all[:, cols], ones[:], alphas_row[:, cols],
                                 start=True, stop=True).then_inc(alphas_spread, 1)
            pe.wait_ge(bias_loaded, DMA_DONE)
            for b in range(BANKS):
                cols = slice(b * BANK, (b + 1) * BANK)
                nc.tensor.matmul(bias_all[:, cols], ones[:], bias_row[:, cols],
                                 start=True, stop=True).then_inc(bias_spread, 1)

        @block.vector
        def _(dve):
            def dots(n, s):
                dve.wait_ge(x_loaded[s], n * DMA_DONE + DMA_DONE)
                for r in range(ROWS):
                    nc.vector.tensor_tensor_reduce(
                        out=products[:, r], in0=x_tiles[:, s, r], in1=alphas_all[:], scale=1.0,
                        scalar=0.0, op0=ALU.mult, op1=ALU.add,
                        accum_out=scales[:, s, r:r + 1]).then_inc(dots_done, 1)

            def shifts(s):
                for r in range(ROWS):
                    nc.vector.tensor_tensor(x_tiles[:, s, r], x_tiles[:, s, r], bias_all[:],
                                            ALU.add).then_inc(shifts_done, 1)

            def mixes(n, s):
                dve.wait_ge(init_loaded[s], n * DMA_DONE + DMA_DONE)
                for r in range(ROWS):
                    slices = n * (SLOTS * ROWS) + (s * ROWS + r + 1)
                    dve.wait_ge(dots_done, slices)
                    dve.wait_ge(shifts_done, slices)
                    nc.vector.scalar_tensor_tensor(
                        out=init_tiles[:, s, r], in0=init_tiles[:, s, r],
                        scalar=scales[:, s, r:r + 1], in1=x_tiles[:, s, r],
                        op0=ALU.mult, op1=ALU.add).then_inc(mixes_done, 1)

            def mix_last():
                dve.wait_ge(dots_done, TILES * ROWS)
                dve.wait_ge(shifts_done, TILES * ROWS)
                for r in range(ROWS):
                    for c in range(PIECES):
                        dve.wait_ge(last_init_loaded[r * PIECES + c], DMA_DONE)
                        nc.vector.scalar_tensor_tensor(
                            out=init_tiles[:, LAST, r, piece(c)], in0=init_tiles[:, LAST, r, piece(c)],
                            scalar=scales[:, LAST, r:r + 1], in1=x_tiles[:, LAST, r, piece(c)],
                            op0=ALU.mult, op1=ALU.add).then_inc(last_mixes_done, 1)

            nc.vector.memset(ones[:], 1.0).then_inc(ones_ready, 1)
            dve.wait_ge(alphas_spread, BANKS)
            dots(0, 0)
            dve.wait_ge(bias_spread, BANKS)
            shifts(0)
            mixes(0, 0)
            for s in range(1, SLOTS):
                dots(0, s)
                shifts(s)
                mixes(0, s)
            with dve.Fori(1, PASSES - 1) as n:
                for s in range(SLOTS):
                    dots(n, s)
                    shifts(s)
                    mixes(n, s)
            for s in range(SLOTS):
                dots(PASSES - 1, s)
                shifts(s)
                if s < LAST:
                    mixes(PASSES - 1, s)
            mix_last()

        @block.scalar
        def _(act):
            def store(n, s):
                act.wait_ge(mixes_done, n * (SLOTS * ROWS) + (s + 1) * ROWS)
                act.dma_start(tile_of(out, n * (SLOTS * TILE_ROWS) + s * TILE_ROWS),
                              init_tiles[:, s]).then_inc(stored[s], DMA_DONE)

            act.dma_start(alphas_row[:], alphas.rearrange("d a -> a d")).then_inc(alphas_loaded, DMA_DONE)
            act.dma_start(bias_row[:], bias.rearrange("(a d) -> a d", a=1)).then_inc(bias_loaded, DMA_DONE)
            with act.Fori(0, PASSES - 1) as n:
                for s in range(SLOTS):
                    store(n, s)
            for s in range(SLOTS - 1):
                store(PASSES - 1, s)
            for r in range(ROWS):
                for c in range(PIECES):
                    act.wait_ge(last_mixes_done, r * PIECES + c + 1)
                    act.dma_start(tile_of(out, LAST_ROW0)[:, r, piece(c)],
                                  init_tiles[:, LAST, r, piece(c)]).then_inc(last_stored, DMA_DONE)
            for s in range(SLOTS):
                act.wait_ge(stored[s], (PASSES if s < LAST else PASSES - 1) * DMA_DONE)
            act.wait_ge(last_stored, ROWS * PIECES * DMA_DONE)


_INS = ['r_initial', 'r_X', 'L0_rec_alphas', 'L0_rec_bias']
_OUTS = [((16384, 2048), 'float32')]


def kernel(**inputs):
    import numpy as _np
    import concourse.bacc as _bacc
    from concourse import mybir as _mybir
    from concourse.bass_utils import run_bass_kernel_spmd as _run

    nc = _bacc.Bacc("TRN2", target_bir_lowering=False, num_devices=1)
    arrays, args = {}, []
    for name in _INS:
        a = _np.ascontiguousarray(inputs[name])
        arrays[f"in_{name}_dram"] = a
        args.append(nc.dram_tensor(f"in_{name}_dram", a.shape, _mybir.dt.from_np(a.dtype), kind="ExternalInput").ap())
    for i, (shape, dtype) in enumerate(_OUTS):
        dt = _mybir.dt.from_np(_np.dtype(dtype))
        args.append(nc.dram_tensor(f"out_{i}_dram", shape, dt, kind="ExternalOutput").ap())
    rec_scale_program(nc, *args)
    r = _run(nc, [arrays], core_ids=[0])
    got = tuple(r.results[0][f"out_{i}_dram"] for i in range(len(_OUTS)))
    return got[0]
```
